# Optimizing a Trainium2 kernel written in Bass

```python
import numpy as np
import jax
import jax.numpy as jnp

def _softmax(x, axis=-1):
    return jax.nn.softmax(x, axis=axis)

def _gelu(x):
    return jax.nn.gelu(x, approximate=True)

def _silu(x):
    return jax.nn.silu(x)

def _sigmoid(x):
    return jax.nn.sigmoid(x)

def _layernorm(x, axis=-1, eps=1e-05):
    m = jnp.mean(x, axis=axis, keepdims=True)
    v = jnp.var(x, axis=axis, keepdims=True)
    return (x - m) / jnp.sqrt(v + eps)

def _scatter_add(tgt, idx, src, axis=0):
    return tgt.at[idx].add(src)

def _segment_sum(src, seg, n):
    return jax.ops.segment_sum(src, seg, n)
kernel_name = 'mk_xattn_seq_d1_seqx_r2_2eca50'

def setup_inputs(seed: int=0):
    np.random.seed(seed)
    _w = jnp.asarray

    def _rec_inputs():
        import jax
        import jax.numpy as jnp
        _rk = jax.random.key(seed)
        x = -0.000296 + 1 * jax.random.normal(jax.random.fold_in(_rk, 1), (32, 256, 640), jnp.float32)
        _lenS = 256 - jax.random.randint(jax.random.fold_in(_rk, 7), (32,), 0, max(1, 256 // 4) + 1, jnp.int32)
        _lenS2 = 256 - jax.random.randint(jax.random.fold_in(_rk, 8), (32,), 0, max(1, 256 // 4) + 1, jnp.int32)
        _ctx_2048P = jax.random.normal(jax.random.fold_in(_rk, 11), (32, 16, 1024), jnp.float32)
        _ctx_2048c = jax.random.dirichlet(jax.random.fold_in(_rk, 511), 0.3 * jnp.ones((16,), jnp.float32), (32, 256))
        _ctx_2048t = jnp.einsum('bsk,bkd->bsd', _ctx_2048c, _ctx_2048P)
        _ctx_2048t = _ctx_2048t * jax.lax.rsqrt(jnp.mean(jnp.square(_ctx_2048t)) + 1e-12) * 0.953939
        ctx_2048 = 0.00118529 + 0.99962 * (_ctx_2048t + 0.3 * jax.random.normal(jax.random.fold_in(_rk, 611), (32, 256, 1024), jnp.float32))
        fside_Bx4x4_0 = jax.random.uniform(jax.random.fold_in(_rk, 12), (32, 4, 4), jnp.float32, 0.0, 0.981965)
        return (x, ctx_2048, fside_Bx4x4_0)
    x, ctx_2048, fside_Bx4x4_0 = _rec_inputs()

    def _L0_xattn_setup():
        import jax, jax.numpy as jnp
        import numpy as np
        HEADS = 20
        NUM_IP_TOKENS = 4
        NUM_DUMMY_TOKENS = 4
        IP_SCALE = 1.0
        ASPECT_RATIO = 1.0
        NEG = -10000.0

        def _grid_hw(seq_len, aspect_ratio):
            width = int((seq_len / aspect_ratio) ** 0.5)
            height = seq_len // width
            while width * height != seq_len:
                if width * height < seq_len:
                    width += 1
                else:
                    width -= 1
                height = seq_len // width
            return (height, width)

        def _sdpa(q, k, v, mask=None):
            dh = q.shape[-1]
            scores = jnp.einsum('bhqd,bhkd->bhqk', q, k) / jnp.sqrt(jnp.asarray(dh, q.dtype))
            if mask is not None:
                scores = scores + mask
            probs = jax.nn.softmax(scores, axis=-1)
            return jnp.einsum('bhqk,bhkd->bhqd', probs, v)

        def _split_heads(x, heads):
            b, l, d = x.shape
            return x.reshape(b, l, heads, d // heads).transpose(0, 2, 1, 3)

        def _merge_heads(x):
            b, h, l, dh = x.shape
            return x.transpose(0, 2, 1, 3).reshape(b, l, h * dh)

        def _ip_mask(bbox, batch_size, seq_len, dtype):
            M = bbox.shape[1]
            height, width = _grid_hw(seq_len, ASPECT_RATIO)
            x = jnp.linspace(0.0, 1.0, width, dtype=dtype)
            y = jnp.linspace(0.0, 1.0, height, dtype=dtype)
            yg, xg = jnp.meshgrid(y, x, indexing='ij')
            xg = xg.reshape(-1)
            yg = yg.reshape(-1)
            x1, y1, x2, y2 = (bbox[..., 0:1], bbox[..., 1:2], bbox[..., 2:3], bbox[..., 3:4])
            inside = (xg >= x1) & (xg <= x2) & (yg >= y1) & (yg <= y2)
            ip_mask = jnp.where(inside, 0.0, NEG).astype(dtype)
            ip_mask = jnp.transpose(ip_mask, (0, 2, 1))[:, None]
            ip_mask = jnp.repeat(ip_mask, NUM_IP_TOKENS // M, axis=-1)
            dummy = jnp.where(jnp.any(inside, axis=1), NEG, 0.0).astype(dtype)
            dummy = jnp.repeat(dummy[:, None, :, None], NUM_DUMMY_TOKENS, axis=-1)
            return jnp.concatenate([dummy, ip_mask], axis=-1)
        key = jax.random.key(seed)
        ks = jax.random.split(key, 12)
        B, S, D, C = (4, 2048, 640, 1024)
        text_len, M = (77, 4)
        hidden_states = jax.random.normal(ks[0], (B, S, D), jnp.float32)
        encoder_hidden_states = jax.random.normal(ks[1], (B, text_len + NUM_IP_TOKENS + NUM_DUMMY_TOKENS, C), jnp.float32)
        p1 = jax.random.uniform(ks[2], (B, M, 2), jnp.float32)
        p2 = jax.random.uniform(ks[3], (B, M, 2), jnp.float32)
        bbox = jnp.concatenate([jnp.minimum(p1, p2), jnp.maximum(p1, p2)], axis=-1)
        s = 0.02
        w_q = jax.random.normal(ks[4], (D, D), jnp.float32) * s
        w_k = jax.random.normal(ks[5], (C, D), jnp.float32) * s
        w_v = jax.random.normal(ks[6], (C, D), jnp.float32) * s
        w_k_ip = jax.random.normal(ks[7], (C, D), jnp.float32) * s
        w_v_ip = jax.random.normal(ks[8], (C, D), jnp.float32) * s
        w_out = jax.random.normal(ks[9], (D, D), jnp.float32) * s
        b_out = jnp.zeros((D,), jnp.float32)
        return {'hidden_states': hidden_states, 'encoder_hidden_states': encoder_hidden_states, 'bbox': bbox, 'w_q': w_q, 'w_k': w_k, 'w_v': w_v, 'w_k_ip': w_k_ip, 'w_v_ip': w_v_ip, 'w_out': w_out, 'b_out': b_out}
    _L0_xattn_all = _L0_xattn_setup()
    _L0_xattn_in = {k: v for k, v in _L0_xattn_all.items() if k in ('w_q', 'w_k', 'w_v', 'w_k_ip', 'w_v_ip', 'w_out', 'b_out')}
    del _L0_xattn_all
    return {'x': x, 'ctx_2048': ctx_2048, 'fside_Bx4x4_0': fside_Bx4x4_0, 'L0_xattn_w_q': _L0_xattn_in['w_q'], 'L0_xattn_w_k': _L0_xattn_in['w_k'], 'L0_xattn_w_v': _L0_xattn_in['w_v'], 'L0_xattn_w_k_ip': _L0_xattn_in['w_k_ip'], 'L0_xattn_w_v_ip': _L0_xattn_in['w_v_ip'], 'L0_xattn_w_out': _L0_xattn_in['w_out'], 'L0_xattn_b_out': _L0_xattn_in['b_out']}

def reference(x, ctx_2048, fside_Bx4x4_0, L0_xattn_w_q, L0_xattn_w_k, L0_xattn_w_v, L0_xattn_w_k_ip, L0_xattn_w_v_ip, L0_xattn_w_out, L0_xattn_b_out):
    import jax
    import jax.numpy as jnp

    def _L0_xattn_ref(hidden_states, encoder_hidden_states, bbox, w_q, w_k, w_v, w_k_ip, w_v_ip, w_out, b_out):
        import jax, jax.numpy as jnp
        import numpy as np
        HEADS = 20
        NUM_IP_TOKENS = 4
        NUM_DUMMY_TOKENS = 4
        IP_SCALE = 1.0
        ASPECT_RATIO = 1.0
        NEG = -10000.0

        def _grid_hw(seq_len, aspect_ratio):
            width = int((seq_len / aspect_ratio) ** 0.5)
            height = seq_len // width
            while width * height != seq_len:
                if width * height < seq_len:
                    width += 1
                else:
                    width -= 1
                height = seq_len // width
            return (height, width)

        def _sdpa(q, k, v, mask=None):
            dh = q.shape[-1]
            scores = jnp.einsum('bhqd,bhkd->bhqk', q, k) / jnp.sqrt(jnp.asarray(dh, q.dtype))
            if mask is not None:
                scores = scores + mask
            probs = jax.nn.softmax(scores, axis=-1)
            return jnp.einsum('bhqk,bhkd->bhqd', probs, v)

        def _split_heads(x, heads):
            b, l, d = x.shape
            return x.reshape(b, l, heads, d // heads).transpose(0, 2, 1, 3)

        def _merge_heads(x):
            b, h, l, dh = x.shape
            return x.transpose(0, 2, 1, 3).reshape(b, l, h * dh)

        def _ip_mask(bbox, batch_size, seq_len, dtype):
            M = bbox.shape[1]
            height, width = _grid_hw(seq_len, ASPECT_RATIO)
            x = jnp.linspace(0.0, 1.0, width, dtype=dtype)
            y = jnp.linspace(0.0, 1.0, height, dtype=dtype)
            yg, xg = jnp.meshgrid(y, x, indexing='ij')
            xg = xg.reshape(-1)
            yg = yg.reshape(-1)
            x1, y1, x2, y2 = (bbox[..., 0:1], bbox[..., 1:2], bbox[..., 2:3], bbox[..., 3:4])
            inside = (xg >= x1) & (xg <= x2) & (yg >= y1) & (yg <= y2)
            ip_mask = jnp.where(inside, 0.0, NEG).astype(dtype)
            ip_mask = jnp.transpose(ip_mask, (0, 2, 1))[:, None]
            ip_mask = jnp.repeat(ip_mask, NUM_IP_TOKENS // M, axis=-1)
            dummy = jnp.where(jnp.any(inside, axis=1), NEG, 0.0).astype(dtype)
            dummy = jnp.repeat(dummy[:, None, :, None], NUM_DUMMY_TOKENS, axis=-1)
            return jnp.concatenate([dummy, ip_mask], axis=-1)
        B, S, D = hidden_states.shape
        residual = hidden_states
        end_pos = encoder_hidden_states.shape[1] - (NUM_IP_TOKENS + NUM_DUMMY_TOKENS)
        text = encoder_hidden_states[:, :end_pos]
        ip_h = encoder_hidden_states[:, end_pos:]
        q = _split_heads(hidden_states @ w_q, HEADS)
        k = _split_heads(text @ w_k, HEADS)
        v = _split_heads(text @ w_v, HEADS)
        out_text = _sdpa(q, k, v)
        out_text = _merge_heads(out_text)
        mask_ip = _ip_mask(bbox, B, S, hidden_states.dtype)
        k_ip = _split_heads(ip_h @ w_k_ip, HEADS)
        v_ip = _split_heads(ip_h @ w_v_ip, HEADS)
        out_ip = _merge_heads(_sdpa(q, k_ip, v_ip, mask=mask_ip))
        out = out_text + IP_SCALE * out_ip
        out = out @ w_out + b_out
        out = out + residual
        return out
    x = _L0_xattn_ref(x, ctx_2048, fside_Bx4x4_0, L0_xattn_w_q, L0_xattn_w_k, L0_xattn_w_v, L0_xattn_w_k_ip, L0_xattn_w_v_ip, L0_xattn_w_out, L0_xattn_b_out)
    return x

_drawn_inputs = setup_inputs


def setup_inputs(seed=0):
    import zlib

    import numpy as np

    out = dict(_drawn_inputs(seed))
    spreads = {'L0_xattn_b_out': (0.0, 0.1)}
    factors = {'L0_xattn_w_k': 3.111}
    for name, (base, spread) in spreads.items():
        noise = np.random.default_rng([zlib.crc32(name.encode()), seed]).standard_normal(out[name].shape)
        drawn = base * np.exp(spread * noise) if base else spread * noise
        out[name] = jnp.asarray(drawn.astype(out[name].dtype))
    for name, factor in factors.items():
        out[name] = (out[name] * factor).astype(out[name].dtype)
    return out
```

```python
from contextlib import ExitStack

import concourse.bass as bass
from concourse import mybir

F32 = mybir.dt.float32
F32R = mybir.dt.float32r
ALU = mybir.AluOpType
ACT = mybir.ActivationFunctionType
AX = mybir.AxisListType

P = 128
HEADS = 20
IP = 8
BOXES = 4
NEG = -10000.0


def started(count):
    return not isinstance(count, int) or count > 0


def decoupled_cross_attention(nc, x, ctx, boxes, w_q, w_k, w_v, w_k_ip, w_v_ip, w_out, b_out, grid, ident, out):
    B, S, D = x.shape
    C = ctx.shape[2]
    DB, CB = D // P, C // P
    DH = D // HEADS
    HC = P // DH
    CHUNKS = HEADS // HC
    QB = S // P
    TEXT = S - IP
    TAIL = TEXT - P
    HALF = D // 2
    UNITS = CHUNKS * QB
    STEPS = UNITS
    SCALE = float(DH) ** -0.5
    STACK_DMAS = 4
    assert QB == 2 and DH == 32 and S == 256 and D % P == 0 and C % P == 0 and B % 2 == 0

    WORK = [
        [("ctxT", 0), ("ctxT", 1), ("q", 0), ("ctxT", 2), ("ctxT", 3)],
        [("k", 0)],
        [("v", 0, 0)],
        [("q", 1), ("k", 1)],
        [("v", 1, 0)],
        [("q", 2), ("k", 2)],
        [("v", 0, 1)],
        [("q", 3), ("k", 3)],
        [("v", 1, 1)],
        [("q", 4), ("k", 4), ("xT", 0), ("xT", 1), ("xT", 2)],
    ]
    AHEAD_OF_EXP = [2, 0, 0, 0, 0, 0, 0, 0, 0, 0]
    AHEAD_OF_SUMS = [2, 0, 0, 1, 0, 1, 0, 1, 0, 1]
    AHEAD_OF_PV = [len(step) for step in WORK[:-1]] + [2]
    ORDER = [item for step in WORK for item in step]
    ITEMS = len(ORDER)
    HI_ITEMS = sum(item[0] != "v" for item in ORDER)
    SETUP = ([("ctxT", g) for g in range(4)] + [("xT", g) for g in range(3)] + [("k_ip", c) for c in range(CHUNKS)]
             + [("v", tb, half) for half in range(2) for tb in range(QB)])
    SETUP_HI = sum(item[0] != "v" for item in SETUP)
    KEYS_IP = SETUP.index(("v", 0, 0))
    RING = 3
    assert ITEMS % RING == 0

    ROWS_K_IP, ROWS_V_IP, ROWS_Q = CB, 2 * CB, 2 * CB + DB
    ROWS_K, ROWS_V = ROWS_Q + CB, ROWS_Q + 2 * CB
    SETUP_WORK = ([("i", i) for i in range(7)] + [("r", r) for r in range(12)] + [("i", 7)]
                  + [("r", r) for r in range(12, 16)] + [("i", 8), ("r", 16), ("r", 17), ("i", 9), ("r", 18), ("r", 19),
                     ("i", 10), ("r", 20), ("i", 11), ("r", 21), ("r", 22), ("r", 23), ("i", 12), ("r", 24), ("r", 25),
                     ("r", 26), ("i", 13), ("r", 27), ("r", 28), ("i", 14), ("i", 15)] + [("r", r) for r in range(29, 37)])
    assert (CB, DB) == (8, 5)

    def item_number(b, item):
        return len(SETUP) + ITEMS * b + ORDER.index(item)

    def bank(item):
        return (len(SETUP) + ORDER.index(item)) % RING

    def hi_count(b, item):
        return SETUP_HI + HI_ITEMS * b + sum(o[0] != "v" for o in ORDER[:ORDER.index(item)]) + 1

    def chunk_number(b, c):
        return CHUNKS * b + c

    def ring_count(b, odd, c, inc):
        slot = (odd + c) % 2
        return inc // 2 * (CHUNKS * b + c - slot) + inc

    def unit_at(b, odd, s, lag, prev, cur):
        if s >= lag:
            return (b, odd, s - lag) if cur else None
        return (b - 1, 1 - odd, s - lag + UNITS) if prev else None

    def chunk_at(b, odd, s, lag, prev, cur):
        got = unit_at(b, odd, s, lag, prev, cur)
        return (*got[:2], got[2] // 2) if got and got[2] % 2 == 0 else None

    def sweep(engine, period, apart=1):
        for b in range(apart):
            period(b, b % 2, b > 0, True)
        with engine.Fori(0, (B - 1 - apart) // 2) as pair:
            period(2 * pair + apart, 1, True, True)
            period(2 * pair + apart + 1, 0, True, True)
        period(B - 1, 1, True, True)
        period(B, 0, True, False)

    def first(b):
        return isinstance(b, int) and b == 0

    def last(b):
        return isinstance(b, int) and b == B - 1

    attn_dram = nc.dram_tensor("attn_dram", (B, P, CHUNKS, S), F32, kind="Internal").ap()
    v_ip_dram = nc.dram_tensor("v_ip_dram", (B * IP, D), F32, kind="Internal").ap()

    with ExitStack() as held:
        def sb(name, shape, dt=F32):
            return held.enter_context(nc.sbuf_tensor(name, shape, dt))

        def psum(name, shape):
            return held.enter_context(nc.psum_tensor(name, shape, F32))

        def sem(name):
            return held.enter_context(nc.semaphore(name))

        wq_hi, wq_lo = sb("wq_hi", [P, DB, D], F32R), sb("wq_lo", [P, DB, D], F32R)
        wk_hi, wk_lo = sb("wk_hi", [P, CB, D], F32R), sb("wk_lo", [P, CB, D], F32R)
        wv_hi, wv_lo = sb("wv_hi", [P, CB, D], F32R), sb("wv_lo", [P, CB, D], F32R)
        x_in = sb("x_in", [P, QB, D])
        ctx_in = sb("ctx_in", [P, QB, C])
        xT_hi, xT_lo = sb("xT_hi", [P, DB, S], F32R), sb("xT_lo", [P, DB, S], F32R)
        cT_hi, cT_lo = sb("cT_hi", [P, CB, S], F32R), sb("cT_lo", [P, CB, S], F32R)
        v = sb("v", [P, QB, D])
        kip = sb("kip", [P, CHUNKS, 2, B * IP], F32R)
        qk = sb("qk", [P, 2, 4, S], F32R)
        stacked = sb("stacked", [P, 2, HC, 2, S], F32R)
        work = sb("work", [P, 4 * HC * S])
        probs = work[:, 0:2 * HC * S].rearrange("p (r h k) -> p r h k", r=2, h=HC)
        probsT = work[:, 2 * HC * S:4 * HC * S].rearrange("p (t h q) -> p t h q", t=QB, h=HC)
        STAGES = (4 * HC * S) // D
        attnT = sb("attnT", [P, 2, S])
        box = attnT[:, :, :].rearrange("p r s -> p (r s)").rearrange("p (b m k) -> p b m k", m=BOXES, k=4)
        mask = sb("mask", [P, B, QB, IP])
        any_box = sb("any_box", [P, QB, B])
        grid_sb = sb("grid_sb", [P, QB, 2])
        ident_sb = sb("ident_sb", [P, P])
        bias_sb = sb("bias_sb", [P, D])
        ip_scores, ip_shifted = sb("ip_scores", [P, 2, HC, IP]), sb("ip_shifted", [P, 2, HC, IP])
        neg_max, neg_max_ip = sb("neg_max", [P, 2, HC]), sb("neg_max_ip", [P, 2, HC])
        sums, inv_sums = sb("sums", [P, 2, 2, HC]), sb("inv_sums", [P, 2, 2, HC])

        wo_hi, wo_lo = wq_hi, wq_lo
        wo_stage = ([ctx_in[:, :, :].rearrange("p t c -> p (t c)")[:, n * D:(n + 1) * D] for n in range(3)]
                    + [x_in[:, n, :] for n in range(2)])
        attn_in = [x_in[:, :, :].rearrange("p t d -> p (t d)"), v[:, :, :].rearrange("p t d -> p (t d)")]
        attn_hi = [t[:, 0:DB, :].rearrange("p c q -> p (c q)") for t in (xT_hi, cT_hi)]
        attn_lo = [t[:, 0:DB, :].rearrange("p c q -> p (c q)") for t in (xT_lo, cT_lo)]
        residual = [work[:, n * QB * D:(n + 1) * QB * D].rearrange("p (t d) -> p t d", t=QB) for n in range(2)]
        out_sb = [work[:, 2 * QB * D:3 * QB * D].rearrange("p (t d) -> p t d", t=QB),
                  ctx_in[:, :, :].rearrange("p t c -> p (t c)")[:, 0:QB * D].rearrange("p (t d) -> p t d", t=QB)]

        acc = psum("acc", [P, RING, 512])
        scores = psum("scores", [P, HC, S])
        pT = psum("pT", [P, QB, HC, P])
        pv = psum("pv", [P, 512])
        out_acc = ([scores[:, 2 * n:2 * n + 2, :].rearrange("p h k -> p (h k)")[:, 0:HALF] for n in range(2)]
                   + [pT[:, n, :, :].rearrange("p h q -> p (h q)")[:, 0:HALF] for n in range(2)])

        W_ROWS = [(w, hi, lo, r) for w, hi, lo, n in (
            (w_k_ip, wk_hi, wk_lo, CB), (w_v_ip, wv_hi, wv_lo, CB), (w_q, wq_hi, wq_lo, DB), (w_k, wk_hi, wk_lo, CB),
            (w_v, wv_hi, wv_lo, CB)) for r in range(n)]

        def stage(n):
            whole = work[:, (n % STAGES) * D:(n % STAGES + 1) * D]
            return by_head(whole, False) if n < ROWS_K_IP or ROWS_V_IP <= n < ROWS_K else whole

        def split_row(n, part):
            _, hi, lo, r = W_ROWS[n]
            whole = (hi, lo)[part][:, r, :]
            return by_head(whole, True) if n < ROWS_K_IP or ROWS_V_IP <= n < ROWS_K else whole

        def by_head(row, permuted):
            if permuted:
                return row.rearrange("p (c d h) -> p c h d", h=HC, d=DH)
            return row.rearrange("p (c h d) -> p c h d", h=HC, d=DH)

        const_in, bias_in, box_in = sem("const_in"), sem("bias_in"), sem("box_in")
        stage_in = [sem(f"stage_in{i}") for i in range(STAGES)]
        w_hi, w_split = sem("w_hi"), sem("w_split")
        mask_step = sem("mask_step")
        ctx_ip_loaded, ctx_loaded, x_loaded = sem("ctx_ip_loaded"), sem("ctx_loaded"), sem("x_loaded")
        v_ip_saved, v_ip_loaded = sem("v_ip_saved"), sem("v_ip_loaded")
        acc_full = sem("acc_full")
        hi_done = sem("hi_done")
        acc_free = sem("acc_free")
        kip_copied = sem("kip_copied")
        stack_in = [sem(f"stack_in{i}") for i in range(2)]
        scores_done = sem("scores_done")
        max_done = sem("max_done")
        ip_step = sem("ip_step")
        exp_done, exp_ip_done = sem("exp_done"), sem("exp_ip_done")
        inv_done = sem("inv_done")
        norm_done = sem("norm_done")
        pT_done = sem("pT_done")
        pT_out_act, pT_out_dve = sem("pT_out_act"), sem("pT_out_dve")
        pv_done, pv_out = sem("pv_done"), sem("pv_out")
        attn_saved = [sem(f"attn_saved{i}") for i in range(2)]
        wo_in, wo_hi_done, wo_split = sem("wo_in"), sem("wo_hi_done"), sem("wo_split")
        attn_loaded = [sem(f"attn_loaded{i}") for i in range(2)]
        res_loaded = [sem(f"res_loaded{i}") for i in range(2)]
        attn_hi_done, attn_split, res_ready = sem("attn_hi_done"), sem("attn_split"), sem("res_ready")
        out_full, out_ready = sem("out_full"), sem("out_ready")
        out_saved = [sem(f"out_saved{i}") for i in range(2)]

        def in_blocks(t):
            return t.rearrange("(t p) d -> p t d", p=P)

        with nc.Block() as block:
            @block.sync
            def _(sp):
                for n in range(QB):
                    sp.dma_start(ctx_in[:, n, :], ctx[n * B // QB:(n + 1) * B // QB, TEXT:S, :]) \
                        .then_inc(ctx_ip_loaded, 16)
                sp.dma_start(ident_sb[:, :], ident).then_inc(const_in, 16)
                sp.dma_start(grid_sb[:, :, :], grid).then_inc(const_in, 16)
                sp.dma_start(box[:, :, :, :].rearrange("p b m k -> p (b m k)"), boxes.rearrange(
                    "b m k -> (b m k)").unsqueeze(0).to_broadcast([P, B * BOXES * 4])).then_inc(box_in, 16)
                sp.dma_start(x_in[:, :, :], in_blocks(x[0])).then_inc(x_loaded, 16)
                for n, (w, _, _, r) in enumerate(W_ROWS):
                    if n >= STAGES:
                        sp.wait_ge(w_split, n - STAGES + 1)
                    sp.dma_start(work[:, (n % STAGES) * D:(n % STAGES + 1) * D], w[r * P:(r + 1) * P, :]).then_inc(stage_in[n % STAGES], 16)
                    if n == 15:
                        sp.wait_ge(acc_full, 7)
                        sp.dma_start(ctx_in[:, :, :], in_blocks(ctx[0])).then_inc(ctx_loaded, 16)
                        sp.dma_start(x_in[:, :, :], in_blocks(x[1])).then_inc(x_loaded, 16)
                sp.dma_start(bias_sb[:, :], b_out.unsqueeze(0).to_broadcast([P, D])).then_inc(bias_in, 16)
                sp.wait_ge(acc_free, len(SETUP))
                sp.dma_start(in_blocks(v_ip_dram), v[:, :, :]).then_inc(v_ip_saved, 16)
                sp.wait_ge(v_ip_saved, 16)
                sp.dma_start(v[TAIL:P, 1, :], v_ip_dram[0:IP, :]).then_inc(v_ip_loaded, 16)

                def period(b, odd, prev, cur):
                    for s in range(STEPS):
                        got = chunk_at(b, odd, s, 8, prev, cur)
                        if got:
                            cb, co, c = got
                            slot = (co + c) % 2
                            sp.wait_ge(pv_out, chunk_number(cb, c) + 1)
                            sp.dma_start(attn_dram[cb, :, c, :], attnT[:, slot, :]).then_inc(attn_saved[slot], 16)
                        if s == 0 and cur and not first(b) and not last(b):
                            sp.wait_ge(acc_full, item_number(b - 1, ("xT", 2)) + 1)
                            sp.dma_start(x_in[:, :, :], in_blocks(x[b + 1])).then_inc(x_loaded, 16)
                        if s == 1 and cur and not last(b):
                            sp.wait_ge(acc_full, item_number(b, ("ctxT", 3)) + 1)
                            sp.dma_start(ctx_in[:, :, :], in_blocks(ctx[b + 1])).then_inc(ctx_loaded, 16)
                        if s == 6 and cur and not first(b):
                            sp.wait_ge(pv_done, CHUNKS * b)
                            sp.dma_start(v[TAIL:P, 1, :], v_ip_dram[bass.ds(b * IP, IP), :]).then_inc(v_ip_loaded, 16)
                        for item in WORK[s] if cur else []:
                            if item[0] != "k":
                                continue
                            c = item[1]
                            slot = (odd + c) % 2
                            g = chunk_number(b, c)
                            sp.wait_ge(kip_copied, g + 1)
                            for t in range(4):
                                q_part, k_part = t // 2, 2 + t % 2
                                sp.dma_start(stacked[DH * t:DH * (t + 1), slot, :, :, :].bitcast(F32),
                                             qk[:, slot, q_part:k_part + 1:k_part - q_part, :].bitcast(F32)
                                             ).then_inc(stack_in[slot], 16)
                        if last(b) and s == 9:
                            sp.wait_ge(acc_full, item_number(b, ("ctxT", 3)) + 1)
                            for n in range(DB):
                                sp.dma_start(wo_stage[n], w_out[n * P:(n + 1) * P, :]).then_inc(wo_in, 16)
                        if not cur and s == 5:
                            sp.wait_ge(wo_split, DB)
                            sp.dma_start(attn_in[0], attn_dram[0].rearrange("p c q -> p (c q)")) \
                                .then_inc(attn_loaded[0], 16)
                            sp.wait_ge(pT_done, UNITS * B)
                            sp.dma_start(residual[0], in_blocks(x[0])).then_inc(res_loaded[0], 16)

                sweep(sp, period)

                for slot in range(2):
                    sp.wait_ge(attn_saved[slot], 16 * (B * CHUNKS // 2))

                def out_period(b, odd, prev, cur):
                    if cur and not first(b):
                        if started(b - 1):
                            sp.wait_ge(attn_split, b - 1)
                        sp.dma_start(attn_in[odd], attn_dram[b].rearrange("p c q -> p (c q)")) \
                            .then_inc(attn_loaded[odd], 16)
                        if started(b - 1):
                            sp.wait_ge(out_ready, 4 * (b - 1))
                        sp.dma_start(residual[odd], in_blocks(x[b])).then_inc(res_loaded[odd], 16)

                sweep(sp, out_period, apart=3)

            @block.gpsimd
            def _(pool):
                def period(b, odd, prev, cur):
                    for s in range(STEPS):
                        got = unit_at(b, odd, s, 4, prev, cur)
                        if got:
                            ub, _, u = got
                            n = UNITS * ub + u
                            pool.wait_ge(inv_done, n + 1)
                            for part, (lo, hi) in enumerate([(0, TEXT), (TEXT, S)]):
                                some = probs[:, u % 2, :, lo:hi]
                                inv = inv_sums[:, u % 2, part, :].unsqueeze(2).to_broadcast([P, HC, hi - lo])
                                nc.gpsimd.tensor_tensor(some, some, inv, ALU.mult).then_inc(norm_done, 1)

                sweep(pool, period)
                pool.wait_ge(bias_in, 16)

                def out_period(b, odd, prev, cur):
                    if cur:
                        pool.wait_ge(res_loaded[odd], 8 * (b - odd) + 16)
                        nc.gpsimd.tensor_tensor(residual[odd], residual[odd],
                                                bias_sb[:, :].unsqueeze(1).to_broadcast([P, QB, D]), ALU.add) \
                            .then_inc(res_ready, 1)

                sweep(pool, out_period, apart=3)

            def hi_of(odd, item):
                kind, n = item[0], item[1]
                if kind in ("xT", "ctxT"):
                    hi, lo, blocks = (xT_hi, xT_lo, DB) if kind == "xT" else (cT_hi, cT_lo, CB)
                    at, end = 2 * n * S, min(2 * n + 2, blocks) * S
                    return [t[:, :, :].rearrange("p c s -> p (c s)")[:, at:end] for t in (hi, lo)], end - at
                if kind == "k_ip":
                    return [kip[:, n, part, :] for part in range(2)], B * IP
                slot, at = (odd + n) % 2, 0 if kind == "q" else 2
                width = S if kind == "q" else TEXT
                return [qk[:, slot, at + part, 0:width] for part in range(2)], width

            @block.scalar
            def _(act):
                for kind, n in SETUP_WORK:
                    if kind == "r":
                        if n == ROWS_Q:
                            act.wait_ge(acc_full, KEYS_IP)
                        if n == ROWS_K:
                            act.wait_ge(acc_full, len(SETUP))
                        act.wait_ge(stage_in[n % STAGES], 16 * (n // STAGES + 1))
                        nc.scalar.activation(split_row(n, 0), stage(n), ACT.Copy).then_inc(w_hi, 1)
                    elif SETUP[n][0] != "v":
                        (hi, _), width = hi_of(0, SETUP[n])
                        act.wait_ge(acc_full, n + 1)
                        nc.scalar.activation(hi, acc[:, n % RING, 0:width], ACT.Copy).then_inc(hi_done, 1)

                def split_hi(b, odd, item):
                    if item[0] == "v" or (item[0] == "xT" and last(b)):
                        return
                    (hi, _), width = hi_of(odd, item)
                    act.wait_ge(acc_full, item_number(b, item) + 1)
                    if item[0] in "qk" and started(ring_count(b, odd, item[1], 16 * STACK_DMAS) - 16 * STACK_DMAS):
                        act.wait_ge(stack_in[(odd + item[1]) % 2],
                                    ring_count(b, odd, item[1], 16 * STACK_DMAS) - 16 * STACK_DMAS)
                    nc.scalar.activation(hi, acc[:, bank(item), 0:width], ACT.Copy,
                                         scale=SCALE if item[0] == "q" else 1.0).then_inc(hi_done, 1)

                def period(b, odd, prev, cur):
                    for s in range(STEPS):
                        got = chunk_at(b, odd, s, 8, prev, cur)
                        if got:
                            cb, co, c = got
                            act.wait_ge(pv_done, chunk_number(cb, c) + 1)
                            if started(ring_count(cb, co, c, 16) - 16):
                                act.wait_ge(attn_saved[(co + c) % 2], ring_count(cb, co, c, 16) - 16)
                            nc.scalar.activation(attnT[:, (co + c) % 2, :], pv[:, 0:S], ACT.Copy).then_inc(pv_out, 1)
                        got = unit_at(b, odd, s, 6, prev, cur)
                        if got:
                            ub, _, u = got
                            act.wait_ge(pT_done, UNITS * ub + u + 1)
                            if u % 2 == 0 and started(chunk_number(ub, u // 2)):
                                act.wait_ge(pv_done, chunk_number(ub, u // 2))
                            nc.scalar.activation(probsT[:, 0, :, (u % 2) * P:(u % 2 + 1) * P], pT[:, 0, :, :],
                                                 ACT.Copy).then_inc(pT_out_act, 1)
                        items = WORK[s] if cur else []
                        for item in items[:AHEAD_OF_EXP[s]]:
                            split_hi(b, odd, item)
                        got = unit_at(b, odd, s, 4, prev, cur)
                        if got:
                            ub, _, u = got
                            n, r = UNITS * ub + u, u % 2
                            act.wait_ge(max_done, n + 1)
                            if started(n - 1):
                                act.wait_ge(pT_done, n - 1)
                            for h in range(HC):
                                ins = nc.scalar.activation(probs[:, r, h, 0:TEXT], scores[:, h, 0:TEXT], ACT.Exp,
                                                           bias=neg_max[:, r, h:h + 1],
                                                           accum_out=sums[:, r, 0, h:h + 1])
                            ins.then_inc(exp_done, 1)
                            act.wait_ge(ip_step, 4 * n + 3)
                            nc.scalar.activation(probs[:, r, :, TEXT:S], ip_shifted[:, r, :, :], ACT.Exp) \
                                .then_inc(exp_ip_done, 1)
                        for item in items[AHEAD_OF_EXP[s]:]:
                            split_hi(b, odd, item)
                        if not cur and s < DB:
                            if s == 0:
                                act.wait_ge(wo_in, 16 * DB)
                                act.wait_ge(acc_full, item_number(B - 1, ("q", 4)) + 1)
                            nc.scalar.activation(wo_hi[:, s, :], wo_stage[s], ACT.Copy).then_inc(wo_hi_done, 1)
                        if not cur and s == 5:
                            attn_leading(0, 0)

                def attn_leading(b, odd):
                    act.wait_ge(attn_loaded[odd], 8 * (b - odd) + 16)
                    if started(b - 1):
                        act.wait_ge(out_full, 4 * (b - 1))
                    nc.scalar.activation(attn_hi[odd], attn_in[odd], ACT.Copy).then_inc(attn_hi_done, 1)

                sweep(act, period)

                def out_period(b, odd, prev, cur):
                    if cur and not first(b):
                        attn_leading(b, odd)
                    if prev:
                        act.wait_ge(out_ready, 4 * b)
                        act.dma_start(in_blocks(out[b - 1]), out_sb[1 - odd]).then_inc(out_saved[1 - odd], 16)

                sweep(act, out_period, apart=3)
                for slot in range(2):
                    act.wait_ge(out_saved[slot], 16 * (B // 2))

            @block.vector
            def _(dve):
                dve.wait_ge(const_in, 32)
                dve.wait_ge(box_in, 16)
                step = 0
                for qb in range(QB):
                    inside = mask[:, :, qb, BOXES:IP]
                    for k, op in ((0, ALU.is_le), (1, ALU.is_le), (2, ALU.is_ge), (3, ALU.is_ge)):
                        at = grid_sb[:, qb, k % 2:k % 2 + 1]
                        if k == 0:
                            nc.vector.tensor_scalar(inside, box[:, :, :, k], at, None, op).then_inc(mask_step, 1)
                        else:
                            dve.wait_ge(mask_step, step)
                            nc.vector.scalar_tensor_tensor(inside, box[:, :, :, k], at, inside, op, ALU.mult) \
                                .then_inc(mask_step, 1)
                        step += 1
                    dve.wait_ge(mask_step, step)
                    nc.vector.tensor_reduce(any_box[:, qb, :], inside, AX.X, ALU.max).then_inc(mask_step, 1)
                    dve.wait_ge(mask_step, step + 1)
                    nc.vector.tensor_scalar(mask[:, :, qb, 0:BOXES], any_box[:, qb, :].unsqueeze(2).to_broadcast(
                        [P, B, BOXES]), NEG, None, ALU.mult).then_inc(mask_step, 1)
                    nc.vector.tensor_scalar(inside, inside, -NEG, NEG, ALU.mult, ALU.add).then_inc(mask_step, 1)
                    step += 3

                for kind, n in SETUP_WORK:
                    if kind == "r":
                        dve.wait_ge(w_hi, n + 1)
                        nc.vector.tensor_tensor(split_row(n, 1), stage(n), split_row(n, 0).bitcast(F32), ALU.subtract) \
                            .then_inc(w_split, 1)
                        continue
                    dve.wait_ge(acc_full, n + 1)
                    if SETUP[n][0] == "v":
                        _, tb, half = SETUP[n]
                        nc.vector.tensor_copy(v[:, tb, half * HALF:(half + 1) * HALF], acc[:, n % RING, 0:HALF]) \
                            .then_inc(acc_free, 1)
                    else:
                        (hi, lo), width = hi_of(0, SETUP[n])
                        dve.wait_ge(hi_done, min(n, KEYS_IP) + 1)
                        nc.vector.tensor_tensor(lo, acc[:, n % RING, 0:width], hi.bitcast(F32), ALU.subtract) \
                            .then_inc(acc_free, 1)

                def split_lo(b, odd, item):
                    source = acc[:, bank(item), :]
                    if item[0] == "xT" and last(b):
                        return
                    if item[0] == "v":
                        _, tb, half = item
                        rows = P if tb == 0 else TAIL
                        dve.wait_ge(acc_full, item_number(b, item) + 1)
                        if first(b):
                            dve.wait_ge(v_ip_saved, 16)
                        else:
                            dve.wait_ge(pv_done, CHUNKS * b - (CHUNKS // 2 if half == 0 else 0))
                        nc.vector.tensor_copy(v[0:rows, tb, half * HALF:(half + 1) * HALF], source[0:rows, 0:HALF]) \
                            .then_inc(acc_free, 1)
                        return
                    (hi, lo), width = hi_of(odd, item)
                    dve.wait_ge(hi_done, hi_count(b, item))
                    if item[0] == "q":
                        nc.vector.scalar_tensor_tensor(lo, source[:, 0:width], SCALE, hi.bitcast(F32), ALU.mult,
                                                       ALU.subtract).then_inc(acc_free, 1)
                    else:
                        nc.vector.tensor_tensor(lo, source[:, 0:width], hi.bitcast(F32), ALU.subtract) \
                            .then_inc(acc_free, 1)
                    if item[0] == "k":
                        c = item[1]
                        if started(QB * (chunk_number(b, c) - 1)):
                            dve.wait_ge(scores_done, QB * (chunk_number(b, c) - 1))
                        nc.vector.tensor_copy(qk[:, (odd + c) % 2, 2:4, TEXT:S],
                                              kip[:, c, :, bass.ds(b * IP, IP)].bitcast(F32)).then_inc(kip_copied, 1)

                def period(b, odd, prev, cur):
                    for s in range(STEPS):
                        unit = unit_at(b, odd, s, 4, prev, cur)
                        if unit:
                            ub, _, u = unit
                            n, r = UNITS * ub + u, u % 2
                            dve.wait_ge(scores_done, n + 1)
                            nc.vector.tensor_tensor(
                                ip_scores[:, r, :, :], scores[:, :, TEXT:S],
                                mask[:, ub, r, :].unsqueeze(1).to_broadcast([P, HC, IP]), ALU.add).then_inc(ip_step, 1)
                            nc.vector.tensor_reduce(neg_max[:, r, :], scores[:, :, 0:TEXT], AX.X, ALU.max,
                                                    negate=True).then_inc(max_done, 1)
                        got = unit_at(b, odd, s, 6, prev, cur)
                        if got:
                            tb, _, t = got
                            dve.wait_ge(pT_done, UNITS * tb + t + 1)
                            if t % 2 == 0 and started(chunk_number(tb, t // 2)):
                                dve.wait_ge(pv_done, chunk_number(tb, t // 2))
                            nc.vector.tensor_copy(probsT[:, 1, :, (t % 2) * P:(t % 2 + 1) * P], pT[:, 1, :, :]) \
                                .then_inc(pT_out_dve, 1)
                        if unit:
                            dve.wait_ge(ip_step, 4 * n + 1)
                            nc.vector.tensor_reduce(neg_max_ip[:, r, :], ip_scores[:, r, :, :], AX.X, ALU.max,
                                                    negate=True).then_inc(ip_step, 1)
                            dve.wait_ge(ip_step, 4 * n + 2)
                            nc.vector.tensor_tensor(
                                ip_shifted[:, r, :, :], ip_scores[:, r, :, :],
                                neg_max_ip[:, r, :].unsqueeze(2).to_broadcast([P, HC, IP]), ALU.add).then_inc(ip_step, 1)
                        items = WORK[s] if cur else []
                        for item in items[:AHEAD_OF_SUMS[s]]:
                            split_lo(b, odd, item)
                        if unit:
                            dve.wait_ge(exp_ip_done, n + 1)
                            nc.vector.tensor_reduce(sums[:, r, 1, :], probs[:, r, :, TEXT:S], AX.X, ALU.add) \
                                .then_inc(ip_step, 1)
                            dve.wait_ge(ip_step, 4 * n + 4)
                            nc.vector.reciprocal(inv_sums[:, r, :, :], sums[:, r, :, :]).then_inc(inv_done, 1)
                        for item in items[AHEAD_OF_SUMS[s]:]:
                            split_lo(b, odd, item)
                        if not cur and s < DB:
                            dve.wait_ge(wo_hi_done, s + 1)
                            nc.vector.tensor_tensor(wo_lo[:, s, :], wo_stage[s], wo_hi[:, s, :].bitcast(F32),
                                                    ALU.subtract).then_inc(wo_split, 1)
                        if not cur and s == 5:
                            attn_rest(0, 0)

                def attn_rest(b, odd):
                    dve.wait_ge(attn_hi_done, b + 1)
                    nc.vector.tensor_tensor(attn_lo[odd], attn_in[odd], attn_hi[odd].bitcast(F32), ALU.subtract) \
                        .then_inc(attn_split, 1)

                sweep(dve, period)

                def out_period(b, odd, prev, cur):
                    if cur and not first(b):
                        attn_rest(b, odd)
                    if prev:
                        slot, o = 1 - odd, b - 1
                        dve.wait_ge(res_ready, o + 1)
                        if started(8 * (o - slot)):
                            dve.wait_ge(out_saved[slot], 8 * (o - slot))
                        for n in range(4):
                            at = (slice(None), n // 2, slice(n % 2 * HALF, (n % 2 + 1) * HALF))
                            dve.wait_ge(out_full, 4 * o + n + 1)
                            nc.vector.tensor_tensor(out_sb[slot][at], out_acc[n], residual[slot][at], ALU.add) \
                                .then_inc(out_ready, 1)

                sweep(dve, out_period, apart=3)

            @block.tensor
            def _(pe):
                def three_passes(to, stationary, moving, blocks, done):
                    for n in range(blocks):
                        for s_part, m_part in ((0, 0), (0, 1), (1, 0)):
                            mm = nc.tensor.matmul(to, stationary(s_part, n), moving(m_part, n),
                                                  start=(n == 0 and s_part == 0 and m_part == 0),
                                                  stop=(n == blocks - 1 and s_part == 1))
                    mm.then_inc(done, 1)

                def run_item(item, to):
                    kind = item[0]
                    if kind in ("xT", "ctxT"):
                        source, blocks = (x_in, DB) if kind == "xT" else (ctx_in, CB)
                        g = item[1]
                        for blk in range(2 * g, min(2 * g + 2, blocks)):
                            for t in range(QB):
                                at = ((blk - 2 * g) * QB + t) * P
                                mm = nc.tensor.transpose(to[:, at:at + P], source[:, t, blk * P:(blk + 1) * P],
                                                         ident_sb[:, :])
                        mm.then_inc(acc_full, 1)
                    elif kind == "q":
                        cols = slice(item[1] * P, (item[1] + 1) * P)
                        three_passes(to[:, 0:S], lambda part, n: (wq_hi, wq_lo)[part][:, n, cols],
                                     lambda part, n: (xT_hi, xT_lo)[part][:, n, :], DB, acc_full)
                    elif kind in ("k", "k_ip"):
                        cols = slice(item[1] * P, (item[1] + 1) * P)
                        width = TEXT if kind == "k" else B * IP
                        three_passes(to[:, 0:width], lambda part, n: (wk_hi, wk_lo)[part][:, n, cols],
                                     lambda part, n: (cT_hi, cT_lo)[part][:, n, 0:width], CB, acc_full)
                    else:
                        _, tb, half = item
                        three_passes(to[:, 0:HALF], lambda part, n: (cT_hi, cT_lo)[part][:, n, tb * P:(tb + 1) * P],
                                     lambda part, n: (wv_hi, wv_lo)[part][:, n, half * HALF:(half + 1) * HALF],
                                     CB, acc_full)

                pe.wait_ge(const_in, 32)
                for n, item in enumerate(SETUP):
                    if item == ("ctxT", 0):
                        pe.wait_ge(ctx_ip_loaded, 16 * QB)
                    if item == ("xT", 0):
                        pe.wait_ge(x_loaded, 16)
                    if item == ("k_ip", 0):
                        pe.wait_ge(w_split, ROWS_K_IP)
                    if item == ("v", 0, 0):
                        pe.wait_ge(w_split, ROWS_V_IP)
                    if n >= RING:
                        pe.wait_ge(acc_free, n - RING + 1)
                    run_item(item, acc[:, n % RING, :])

                def project(b, item):
                    n = item_number(b, item)
                    if item[0] == "xT" and last(b):
                        return
                    pe.wait_ge(acc_free, n - RING + 1)
                    if item == ("ctxT", 0):
                        pe.wait_ge(ctx_loaded, 16 * (b + 1))
                    if item == ("xT", 0):
                        pe.wait_ge(x_loaded, 16 * (b + 2))
                    if item == ("k", 0):
                        pe.wait_ge(acc_free, item_number(b, ("ctxT", 3)) + 1)
                    if first(b) and item in (("q", 0), ("k", 0), ("v", 0, 0)):
                        pe.wait_ge(w_split, {"q": ROWS_Q, "k": ROWS_K, "v": ROWS_V}[item[0]])
                    run_item(item, acc[:, bank(item), :])

                def period(b, odd, prev, cur):
                    for s in range(STEPS):
                        got = unit_at(b, odd, s, 6, prev, cur)
                        if got:
                            ub, _, u = got
                            n = UNITS * ub + u
                            pe.wait_ge(norm_done, 2 * (n + 1))
                            if started(n):
                                pe.wait_ge(pT_out_act, n)
                                pe.wait_ge(pT_out_dve, n)
                            for t in range(QB):
                                for h in range(HC):
                                    mm = nc.tensor.transpose(pT[:, t, h, :], probs[:, u % 2, h, t * P:(t + 1) * P],
                                                             ident_sb[:, :])
                            mm.then_inc(pT_done, 1)
                        items = WORK[s] if cur else []
                        for item in items[:AHEAD_OF_PV[s]]:
                            project(b, item)
                        got = chunk_at(b, odd, s - 1, 6, prev, cur) if s >= 1 else None
                        if got:
                            cb, _, c = got
                            g = chunk_number(cb, c)
                            pe.wait_ge(pT_out_act, QB * (g + 1))
                            pe.wait_ge(pT_out_dve, QB * (g + 1))
                            if c in (0, CHUNKS // 2):
                                pe.wait_ge(acc_free, item_number(cb, ("v", 1, 0 if c == 0 else 1)) + 1)
                            if c == 0:
                                pe.wait_ge(v_ip_loaded, 16 * (cb + 1))
                            if started(g):
                                pe.wait_ge(pv_out, g)
                            for t in range(QB):
                                for h in range(HC):
                                    col = (HC * c + h) * DH
                                    mm = nc.tensor.matmul(pv[DH * h:DH * (h + 1), 0:S], v[:, t, col:col + DH],
                                                          probsT[:, t, h, :], start=(t == 0), stop=(t == QB - 1))
                            mm.then_inc(pv_done, 1)
                        for item in items[AHEAD_OF_PV[s]:]:
                            project(b, item)
                        got = unit_at(b, odd, s, 3, prev, cur)
                        if got:
                            ub, uo, u = got
                            n, slot = UNITS * ub + u, (uo + u // 2) % 2
                            if u % 2 == 0:
                                pe.wait_ge(stack_in[slot], ring_count(ub, uo, u // 2, 16 * STACK_DMAS))
                            if started(n):
                                pe.wait_ge(exp_done, n)
                            for h in range(HC):
                                mm = nc.tensor.matmul(scores[:, h, :], stacked[:, slot, h, 0, (u % 2) * P:(u % 2 + 1) * P],
                                                      stacked[:, slot, h, 1, :], start=True, stop=True)
                            mm.then_inc(scores_done, 1)

                sweep(pe, period)
                pe.wait_ge(wo_split, DB)
                pe.wait_ge(exp_done, UNITS * B)

                def out_period(b, odd, prev, cur):
                    if not cur:
                        return
                    pe.wait_ge(attn_split, b + 1)
                    for n in range(4):
                        t, half = n // 2, n % 2
                        if started(4 * (b - 1) + n + 1) :
                            pe.wait_ge(out_ready, 4 * (b - 1) + n + 1)
                        three_passes(
                            out_acc[n],
                            lambda part, c: (attn_hi, attn_lo)[part][odd][:, c * S + t * P:c * S + (t + 1) * P],
                            lambda part, c: (wo_hi, wo_lo)[part][:, c, half * HALF:(half + 1) * HALF], DB, out_full)

                sweep(pe, out_period, apart=3)


def _grid(side, blocks):
    import numpy as np
    step = np.arange(side - 1, dtype=np.float32) * np.float32(1 / (side - 1))
    line = np.concatenate([step, np.ones(1, np.float32)])
    n = np.arange(side * side)
    both = np.stack([line[n % side], line[n // side]], axis=-1)
    return np.ascontiguousarray(both.reshape(blocks, -1, 2).transpose(1, 0, 2))


_INS = ['x', 'ctx_2048', 'fside_Bx4x4_0', 'L0_xattn_w_q', 'L0_xattn_w_k', 'L0_xattn_w_v', 'L0_xattn_w_k_ip',
        'L0_xattn_w_v_ip', 'L0_xattn_w_out', 'L0_xattn_b_out']


def kernel(**inputs):
    import numpy as _np
    import concourse.bacc as _bacc
    from concourse import mybir as _mybir
    from concourse.bass_utils import run_bass_kernel_spmd as _run

    nc = _bacc.Bacc("TRN2", target_bir_lowering=False, num_devices=1)
    arrays, args = {}, []
    given = {name: _np.ascontiguousarray(inputs[name]) for name in _INS}
    given["grid"] = _grid(16, 2)
    given["ident"] = _np.eye(128, dtype=_np.float32)
    for name, a in given.items():
        arrays[f"in_{name}_dram"] = a
        args.append(nc.dram_tensor(f"in_{name}_dram", a.shape, _mybir.dt.from_np(a.dtype), kind="ExternalInput").ap())
    shape = given["x"].shape
    args.append(nc.dram_tensor("out_0_dram", shape, _mybir.dt.float32, kind="ExternalOutput").ap())
    decoupled_cross_attention(nc, *args)
    r = _run(nc, [arrays], core_ids=[0])
    return r.results[0]["out_0_dram"]
```

```python
from contextlib import ExitStack

import concourse.bass as bass
from concourse import mybir

F32 = mybir.dt.float32
F32R = mybir.dt.float32r
ALU = mybir.AluOpType
ACT = mybir.ActivationFunctionType
AX = mybir.AxisListType

P = 128
HEADS = 20
IP = 8
BOXES = 4
NEG = -10000.0
EXP_AND_LN = 6


def started(count):
    return not isinstance(count, int) or count > 0


def decoupled_cross_attention(nc, x, ctx, boxes, w_q, w_k, w_v, w_k_ip, w_v_ip, w_out, b_out, grid, ident,
                              key_rows, out):
    B, S, D = x.shape
    C = ctx.shape[2]
    DB, CB = D // P, C // P
    DH = D // HEADS
    HC = P // DH
    CHUNKS = HEADS // HC
    QB = S // P
    TEXT = S - IP
    TAIL = TEXT - P
    HALF = D // 2
    UNITS = CHUNKS * QB
    STEPS = UNITS
    SCALE = float(DH) ** -0.5
    STACKS = 3
    PAIRS = ((0, 0), (0, 1), (1, 0))
    ROWS = DH * len(PAIRS)
    SHIFTS = 4 * HC
    assert ROWS + DH == P and SHIFTS + 2 * IP == DH
    assert QB == 2 and DH == 32 and S == 256 and D % P == 0 and C % P == 0 and B % 2 == 0

    WORK = [
        [("ctxT", 0), ("q", 0), ("ctxT", 1), ("ctxT", 2), ("ctxT", 3)],
        [("k", 0)],
        [("v", 0, 0)],
        [("q", 1), ("k", 1)],
        [("v", 1, 0)],
        [("q", 2), ("k", 2)],
        [("v", 0, 1)],
        [("q", 3), ("k", 3)],
        [("v", 1, 1)],
        [("q", 4), ("k", 4), ("xT", 0), ("xT", 1), ("xT", 2)],
    ]
    AHEAD_OF_EXP = [1, 0, 0, 0, 0, 0, 0, 0, 0, 0]
    AHEAD_OF_LOGS = [3, 1, 0, 1, 0, 1, 0, 1, 0, 1]
    DVE_WORK = [WORK[0][:-2], WORK[0][-2:] + WORK[1], *WORK[2:-1], WORK[-1][:-1]]
    AHEAD_OF_SUMS = [1, 2, 0, 1, 0, 1, 0, 1, 0, 1]
    ORDER = [item for step in WORK for item in step]
    ITEMS = len(ORDER)
    HI_ITEMS = sum(item[0] != "v" for item in ORDER)
    SETUP = ([("ctxT", g) for g in range(4)] + [("k_ip", c) for c in range(CHUNKS)] + [("xT", g) for g in range(3)]
             + [("v", tb, half) for half in range(2) for tb in range(QB)])
    SETUP_HI = sum(item[0] != "v" for item in SETUP)
    KEYS_IP = SETUP.index(("v", 0, 0))
    RING = 3
    assert ITEMS % RING == 0

    ROWS_K_IP, ROWS_V_IP, ROWS_Q = CB, 2 * CB, 2 * CB + DB
    ROWS_K, ROWS_V = ROWS_Q + CB, ROWS_Q + 2 * CB
    SETUP_WORK = [("i", i) for i in range(4)]
    for item, rows in ((4, 10), (5, 13), (6, 16), (7, 18), (8, 19), (9, 19), (10, 19), (11, 20), (12, 25), (13, 29)):
        SETUP_WORK += [("r", r) for r in range(sum(kind == "r" for kind, _ in SETUP_WORK), rows)] + [("i", item)]
    SETUP_WORK += [("i", 14), ("i", 15)]
    assert (CB, DB) == (8, 5)

    def item_number(b, item):
        return len(SETUP) + ITEMS * b + ORDER.index(item)

    def bank(item):
        return (len(SETUP) + ORDER.index(item)) % RING

    def hi_count(b, item):
        return SETUP_HI + HI_ITEMS * b + sum(o[0] != "v" for o in ORDER[:ORDER.index(item)]) + 1

    def chunk_number(b, c):
        return CHUNKS * b + c

    def stack_slot(turn, c):
        return (CHUNKS * turn + c) % STACKS

    def stack_count(b, turn, c):
        return 16 * len(PAIRS) // STACKS * (CHUNKS * b + c - stack_slot(turn, c)) + 16 * len(PAIRS)

    def saved_count(b, c):
        return 16 * ((3 - c % 2) * b + c // 2 + 1)

    def unit_at(b, turn, s, lag, prev, cur):
        if s >= lag:
            return (b, turn, s - lag) if cur else None
        return (b - 1, (turn - 1) % STACKS, s - lag + UNITS) if prev else None

    def chunk_at(b, turn, s, lag, prev, cur):
        got = unit_at(b, turn, s, lag, prev, cur)
        return (*got[:2], got[2] // 2) if got and got[2] % 2 == 0 else None

    def sweep(engine, period, apart, turns):
        assert (B - 1 - apart) % turns == 0
        for b in range(apart):
            period(b, b % turns, b > 0, True)
        with engine.Fori(0, (B - 1 - apart) // turns) as i:
            for n in range(apart, apart + turns):
                period(turns * i + n, n % turns, True, True)
        period(B - 1, (B - 1) % turns, True, True)
        period(B, B % turns, True, False)

    def first(b):
        return isinstance(b, int) and b == 0

    def last(b):
        return isinstance(b, int) and b == B - 1

    attn_dram = nc.dram_tensor("attn_dram", (B, P, CHUNKS, S), F32, kind="Internal").ap()
    v_ip_dram = nc.dram_tensor("v_ip_dram", (B * IP, D), F32, kind="Internal").ap()

    with ExitStack() as held:
        def sb(name, shape, dt=F32):
            return held.enter_context(nc.sbuf_tensor(name, shape, dt))

        def psum(name, shape):
            return held.enter_context(nc.psum_tensor(name, shape, F32))

        def sem(name):
            return held.enter_context(nc.semaphore(name))

        wq_hi, wq_lo = sb("wq_hi", [P, DB, D], F32R), sb("wq_lo", [P, DB, D], F32R)
        wk_hi, wk_lo = sb("wk_hi", [P, CB, D], F32R), sb("wk_lo", [P, CB, D], F32R)
        wv_hi, wv_lo = sb("wv_hi", [P, CB, D], F32R), sb("wv_lo", [P, CB, D], F32R)
        x_in = sb("x_in", [P, QB, D])
        ctx_in = sb("ctx_in", [P, QB, C])
        xT_hi, xT_lo = sb("xT_hi", [P, DB, S], F32R), sb("xT_lo", [P, DB, S], F32R)
        cT_hi, cT_lo = sb("cT_hi", [P, CB, S], F32R), sb("cT_lo", [P, CB, S], F32R)
        v = sb("v", [P, QB, D])
        kip = sb("kip", [P, CHUNKS, 2, B * IP], F32R)
        qk = sb("qk", [P, 2, 4, S], F32R)
        SPARE = STACKS * HC * 2 * S
        STAGES = SPARE // D
        with nc.sbuf_tensor("spare", [P, SPARE], F32) as spare:
            pass
        stacked = sb("stacked", [P, STACKS, HC, 2, S], F32R)
        probsT = sb("probsT", [P, QB, HC, S])
        attnT = sb("attnT", [P, 2, S])
        box = attnT[:, :, :].rearrange("p r s -> p (r s)").rearrange("p (b m k) -> p b m k", m=BOXES, k=4)
        mask = sb("mask", [P, B, QB, IP])
        any_box = sb("any_box", [P, QB, B])
        grid_sb = sb("grid_sb", [P, QB, 2])
        ident_sb = sb("ident_sb", [P, P])
        ip_scores, ip_shifted = sb("ip_scores", [P, 2, HC, IP]), sb("ip_shifted", [P, 2, HC, IP])
        neg_max, sums, logs, shift = (sb(name, [P, 2, 2, HC]) for name in ("neg_max", "sums", "logs", "shift"))
        shifts = sb("shifts", [P, 2, DH], F32R)

        wo_hi, wo_lo = wq_hi, wq_lo
        wo_stage = ([ctx_in[:, :, :].rearrange("p t c -> p (t c)")[:, n * D:(n + 1) * D] for n in range(3)]
                    + [x_in[:, n, :] for n in range(2)])
        attn_in = [x_in[:, :, :].rearrange("p t d -> p (t d)"), v[:, :, :].rearrange("p t d -> p (t d)")]
        attn_hi = [t[:, 0:DB, :].rearrange("p c q -> p (c q)") for t in (xT_hi, cT_hi)]
        attn_lo = [t[:, 0:DB, :].rearrange("p c q -> p (c q)") for t in (xT_lo, cT_lo)]
        residual = [spare[:, n * QB * D:(n + 1) * QB * D].rearrange("p (t d) -> p t d", t=QB) for n in range(2)]
        out_sb = [spare[:, n * QB * D:(n + 1) * QB * D].rearrange("p (t d) -> p t d", t=QB) for n in range(2, 4)]
        bias_sb = kip[:, :, :, :].rearrange("p c j s -> p (c j s)").bitcast(F32)[:, 0:D]

        acc = psum("acc", [P, RING, 512])
        scores = psum("scores", [P, HC, S])
        scoresT = psum("scoresT", [P, HC, S])
        pv = psum("pv", [P, 512])
        shiftsT = scoresT[ROWS:P, 0, :]
        out_acc = ([scores[:, 2 * n:2 * n + 2, :].rearrange("p h k -> p (h k)")[:, 0:HALF] for n in range(2)]
                   + [scoresT[:, 2 * n:2 * n + 2, :].rearrange("p h k -> p (h k)")[:, 0:HALF] for n in range(2)])

        W_ROWS = [(w, hi, lo, r) for w, hi, lo, n in (
            (w_k_ip, wk_hi, wk_lo, CB), (w_v_ip, wv_hi, wv_lo, CB), (w_q, wq_hi, wq_lo, DB), (w_k, wk_hi, wk_lo, CB),
            (w_v, wv_hi, wv_lo, CB)) for r in range(n)]

        def stage(n):
            whole = spare[:, (n % STAGES) * D:(n % STAGES + 1) * D]
            return by_head(whole, False) if n < ROWS_K_IP or ROWS_V_IP <= n < ROWS_K else whole

        def split_row(n, part):
            _, hi, lo, r = W_ROWS[n]
            whole = (hi, lo)[part][:, r, :]
            return by_head(whole, True) if n < ROWS_K_IP or ROWS_V_IP <= n < ROWS_K else whole

        def by_head(row, permuted):
            if permuted:
                return row.rearrange("p (c d h) -> p c h d", h=HC, d=DH)
            return row.rearrange("p (c h d) -> p c h d", h=HC, d=DH)

        const_in, bias_in, box_in = sem("const_in"), sem("bias_in"), sem("box_in")
        stage_in = [sem(f"stage_in{i}") for i in range(STAGES)]
        w_hi, w_split = sem("w_hi"), sem("w_split")
        mask_step = sem("mask_step")
        ctx_ip_loaded, ctx_loaded, x_loaded = sem("ctx_ip_loaded"), sem("ctx_loaded"), sem("x_loaded")
        v_ip_saved, v_ip_loaded = sem("v_ip_saved"), sem("v_ip_loaded")
        acc_full = sem("acc_full")
        hi_done = sem("hi_done")
        acc_free = sem("acc_free")
        kip_copied = sem("kip_copied")
        stack_in = [sem(f"stack_in{i}") for i in range(STACKS)]
        scores_done = sem("scores_done")
        max_done = sem("max_done")
        ip_step = sem("ip_step")
        exp_done, exp_ip_done = sem("exp_done"), sem("exp_ip_done")
        logs_done = sem("logs_done")
        shifts_cleared, shift_step = sem("shifts_cleared"), sem("shift_step")
        mask_copied = sem("mask_copied")
        shiftsT_done = sem("shiftsT_done")
        shifts_in = sem("shifts_in")
        key_rows_loaded, key_rows_in = sem("key_rows_loaded"), sem("key_rows_in")
        scoresT_done, probsT_done = sem("scoresT_done"), sem("probsT_done")
        pv_done, pv_out = sem("pv_done"), sem("pv_out")
        attn_saved = [sem(f"attn_saved{i}") for i in range(2)]
        wo_in, wo_hi_done, wo_split = sem("wo_in"), sem("wo_hi_done"), sem("wo_split")
        attn_loaded = [sem(f"attn_loaded{i}") for i in range(2)]
        res_loaded = [sem(f"res_loaded{i}") for i in range(2)]
        attn_hi_done, attn_split, res_ready = sem("attn_hi_done"), sem("attn_split"), sem("res_ready")
        out_full, out_ready = sem("out_full"), sem("out_ready")
        out_saved = [sem(f"out_saved{i}") for i in range(2)]

        def in_blocks(t):
            return t.rearrange("(t p) d -> p t d", p=P)

        with nc.Block() as block:
            @block.sync
            def _(sp):
                for n in range(QB):
                    sp.dma_start(ctx_in[:, n, :], ctx[n * B // QB:(n + 1) * B // QB, TEXT:S, :]) \
                        .then_inc(ctx_ip_loaded, 16)
                sp.dma_start(ident_sb[:, :], ident).then_inc(const_in, 16)
                sp.dma_start(grid_sb[:, :, :], grid).then_inc(const_in, 16)
                sp.dma_start(box[:, :, :, :].rearrange("p b m k -> p (b m k)"), boxes.rearrange(
                    "b m k -> (b m k)").unsqueeze(0).to_broadcast([P, B * BOXES * 4])).then_inc(box_in, 16)
                for n, (w, _, _, r) in enumerate(W_ROWS):
                    if n >= STAGES:
                        sp.wait_ge(w_split, n - STAGES + 1)
                    sp.dma_start(spare[:, (n % STAGES) * D:(n % STAGES + 1) * D], w[r * P:(r + 1) * P, :]) \
                        .then_inc(stage_in[n % STAGES], 16)
                    if n == ROWS_K_IP - 1:
                        sp.dma_start(x_in[:, :, :], in_blocks(x[0])).then_inc(x_loaded, 16)
                    if n == ROWS_V_IP - 1:
                        sp.wait_ge(acc_full, SETUP.index(("ctxT", 3)) + 1)
                        sp.dma_start(ctx_in[:, :, :], in_blocks(ctx[0])).then_inc(ctx_loaded, 16)
                    if n == ROWS_K - 1:
                        sp.wait_ge(acc_full, SETUP.index(("xT", 2)) + 1)
                        sp.dma_start(x_in[:, :, :], in_blocks(x[1])).then_inc(x_loaded, 16)
                sp.dma_start(probsT[ROWS:P, 0, :, :], key_rows).then_inc(key_rows_loaded, 16)
                sp.wait_ge(acc_free, len(SETUP))
                sp.dma_start(in_blocks(v_ip_dram), v[:, :, :]).then_inc(v_ip_saved, 16)
                sp.wait_ge(v_ip_saved, 16)
                sp.dma_start(v[TAIL:P, 1, :], v_ip_dram[0:IP, :]).then_inc(v_ip_loaded, 16)

                def period(b, turn, prev, cur):
                    for s in range(STEPS):
                        got = chunk_at(b, turn, s, 8, prev, cur)
                        if got:
                            cb, _, c = got
                            sp.wait_ge(pv_out, chunk_number(cb, c) + 1)
                            sp.dma_start(attn_dram[cb, :, c, :], attnT[:, c % 2, :]).then_inc(attn_saved[c % 2], 16)
                        if s == 0 and cur and not first(b) and not last(b):
                            sp.wait_ge(acc_full, item_number(b - 1, ("xT", 2)) + 1)
                            sp.dma_start(x_in[:, :, :], in_blocks(x[b + 1])).then_inc(x_loaded, 16)
                        if s == 1 and cur and not last(b):
                            sp.wait_ge(acc_full, item_number(b, ("ctxT", 3)) + 1)
                            sp.dma_start(ctx_in[:, :, :], in_blocks(ctx[b + 1])).then_inc(ctx_loaded, 16)
                        if s == 6 and cur and not first(b):
                            sp.wait_ge(pv_done, CHUNKS * b)
                            sp.dma_start(v[TAIL:P, 1, :], v_ip_dram[bass.ds(b * IP, IP), :]).then_inc(v_ip_loaded, 16)
                        for item in WORK[s] if cur else []:
                            if item[0] != "k":
                                continue
                            c = item[1]
                            slot = stack_slot(turn, c)
                            sp.wait_ge(kip_copied, chunk_number(b, c) + 1)
                            for t, (q_part, k_part) in enumerate(PAIRS):
                                k_part += 2
                                sp.dma_start(stacked[DH * t:DH * (t + 1), slot, :, :, :].bitcast(F32),
                                             qk[:, c % 2, q_part:k_part + 1:k_part - q_part, :].bitcast(F32)
                                             ).then_inc(stack_in[slot], 16)
                        if last(b) and s == 9:
                            sp.wait_ge(acc_full, item_number(b, ("ctxT", 3)) + 1)
                            for n in range(DB):
                                sp.dma_start(wo_stage[n], w_out[n * P:(n + 1) * P, :]).then_inc(wo_in, 16)
                            sp.dma_start(bias_sb[:, :], b_out.unsqueeze(0).to_broadcast([P, D])).then_inc(bias_in, 16)
                        if not cur and s == 5:
                            sp.wait_ge(wo_split, DB)
                            sp.dma_start(attn_in[0], attn_dram[0].rearrange("p c q -> p (c q)")) \
                                .then_inc(attn_loaded[0], 16)
                            sp.wait_ge(scoresT_done, QB * CHUNKS * B)
                            sp.dma_start(residual[0], in_blocks(x[0])).then_inc(res_loaded[0], 16)

                sweep(sp, period, apart=1, turns=STACKS)

                for c in (CHUNKS - 2, CHUNKS - 1):
                    sp.wait_ge(attn_saved[c % 2], saved_count(B - 1, c))

                def out_period(b, odd, prev, cur):
                    if cur and not first(b):
                        if started(b - 1):
                            sp.wait_ge(attn_split, b - 1)
                        sp.dma_start(attn_in[odd], attn_dram[b].rearrange("p c q -> p (c q)")) \
                            .then_inc(attn_loaded[odd], 16)
                        if started(b - 1):
                            sp.wait_ge(out_ready, 4 * (b - 1))
                        sp.dma_start(residual[odd], in_blocks(x[b])).then_inc(res_loaded[odd], 16)

                sweep(sp, out_period, apart=3, turns=2)

            @block.gpsimd
            def _(pool):
                nc.gpsimd.memset(shifts[:, :, :].bitcast(F32), 0.0).then_inc(shifts_cleared, 1)
                pool.wait_ge(key_rows_loaded, 16)
                pool.wait_ge(w_split, len(W_ROWS))
                pool.wait_ge(shifts_cleared, 1)
                for slot in range(STACKS):
                    if slot:
                        pool.wait_ge(key_rows_in, slot)
                    nc.gpsimd.tensor_copy(stacked[ROWS:P, slot, :, 1, :], probsT[ROWS:P, 0, :, :]) \
                        .then_inc(key_rows_in, 1)
                pool.wait_ge(key_rows_in, STACKS)

                def period(b, turn, prev, cur):
                    for s in range(STEPS):
                        got = unit_at(b, turn, s, 4, prev, cur)
                        if got:
                            ub, _, u = got
                            n, r = UNITS * ub + u, u % 2
                            pool.wait_ge(logs_done, n + 1)
                            nc.gpsimd.tensor_tensor(shift[:, r, :, :], neg_max[:, r, :, :], logs[:, r, :, :],
                                                    ALU.subtract).then_inc(shift_step, 1)
                            columns = shifts[:, r, 0:SHIFTS].rearrange("p (k j h) -> p k j h", k=2, j=2)
                            if u % 2 == 0 and started(chunk_number(ub, u // 2)):
                                pool.wait_ge(shiftsT_done, chunk_number(ub, u // 2))
                            nc.gpsimd.tensor_tensor(columns[:, :, 0, :], neg_max[:, r, :, :], logs[:, r, :, :],
                                                    ALU.subtract).then_inc(shift_step, 1)
                            pool.wait_ge(shift_step, 3 * n + 2)
                            nc.gpsimd.tensor_tensor(columns[:, :, 1, :], shift[:, r, :, :],
                                                    columns[:, :, 0, :].bitcast(F32), ALU.subtract) \
                                .then_inc(shift_step, 1)

                sweep(pool, period, apart=1, turns=STACKS)
                pool.wait_ge(bias_in, 16)

                def out_period(b, odd, prev, cur):
                    if cur:
                        pool.wait_ge(res_loaded[odd], 8 * (b - odd) + 16)
                        nc.gpsimd.tensor_tensor(residual[odd], residual[odd],
                                                bias_sb[:, :].unsqueeze(1).to_broadcast([P, QB, D]), ALU.add) \
                            .then_inc(res_ready, 1)

                sweep(pool, out_period, apart=3, turns=2)

            def hi_of(item):
                kind, n = item[0], item[1]
                if kind in ("xT", "ctxT"):
                    hi, lo, blocks = (xT_hi, xT_lo, DB) if kind == "xT" else (cT_hi, cT_lo, CB)
                    at, end = 2 * n * S, min(2 * n + 2, blocks) * S
                    return [t[:, :, :].rearrange("p c s -> p (c s)")[:, at:end] for t in (hi, lo)], end - at
                if kind == "k_ip":
                    return [kip[:, n, part, :] for part in range(2)], B * IP
                slot, at = n % 2, 0 if kind == "q" else 2
                width = S if kind == "q" else TEXT
                return [qk[:, slot, at + part, 0:width] for part in range(2)], width

            @block.scalar
            def _(act):
                nc.scalar.add_instruction(mybir.InstLoadActFuncSet(
                    name=nc.get_next_instruction_name(), act_func_set_id=EXP_AND_LN, engine=mybir.EngineType.Activation))

                def row_hi(n):
                    if n == ROWS_Q:
                        act.wait_ge(acc_full, KEYS_IP)
                    if n == ROWS_K:
                        act.wait_ge(acc_full, len(SETUP))
                    act.wait_ge(stage_in[n % STAGES], 16 * (n // STAGES + 1))
                    nc.scalar.activation(split_row(n, 0), stage(n), ACT.Copy).then_inc(w_hi, 1)

                for kind, n in SETUP_WORK:
                    if kind == "r":
                        row_hi(n)
                    elif SETUP[n][0] != "v":
                        (hi, _), width = hi_of(SETUP[n])
                        act.wait_ge(acc_full, n + 1)
                        nc.scalar.activation(hi, acc[:, n % RING, 0:width], ACT.Copy).then_inc(hi_done, 1)

                def split_hi(b, turn, item):
                    if item[0] == "v" or (item[0] == "xT" and last(b)):
                        return
                    (hi, _), width = hi_of(item)
                    act.wait_ge(acc_full, item_number(b, item) + 1)
                    if item[0] in "qk":
                        c = item[1]
                        if c >= 2:
                            act.wait_ge(stack_in[stack_slot(turn, c - 2)], stack_count(b, turn, c - 2))
                        elif not first(b):
                            c = CHUNKS - 1 - c
                            act.wait_ge(stack_in[stack_slot(turn - 1, c)], stack_count(b - 1, (turn - 1) % STACKS, c))
                    nc.scalar.activation(hi, acc[:, bank(item), 0:width], ACT.Copy,
                                         scale=SCALE if item[0] == "q" else 1.0).then_inc(hi_done, 1)

                def period(b, turn, prev, cur):
                    for s in range(STEPS):
                        transposed = chunk_at(b, turn, s, 7, prev, cur)
                        if transposed and s != 1:
                            probabilities(transposed, 0)
                        attended = chunk_at(b, turn, s, 8, prev, cur)
                        if s != 2:
                            attention(attended)
                        items = WORK[s] if cur else []
                        for item in items[:AHEAD_OF_EXP[s]]:
                            split_hi(b, turn, item)
                        got = unit_at(b, turn, s, 4, prev, cur)
                        if got:
                            ub, _, u = got
                            n, r = UNITS * ub + u, u % 2
                            act.wait_ge(max_done, n + 1)
                            if started(n - 1):
                                act.wait_ge(shift_step, 3 * (n - 1))
                            for h in range(HC):
                                ins = nc.scalar.activation(scores[:, h, 0:TEXT], scores[:, h, 0:TEXT], ACT.Exp,
                                                           bias=neg_max[:, r, 0, h:h + 1],
                                                           accum_out=sums[:, r, 0, h:h + 1])
                            ins.then_inc(exp_done, 1)
                            act.wait_ge(ip_step, 4 * n + 3)
                            nc.scalar.activation(ip_shifted[:, r, :, :], ip_shifted[:, r, :, :], ACT.Exp) \
                                .then_inc(exp_ip_done, 1)
                        if s == 2:
                            attention(attended)
                        for item in items[AHEAD_OF_EXP[s]:AHEAD_OF_LOGS[s]]:
                            split_hi(b, turn, item)
                        if transposed:
                            probabilities(transposed, 1)
                        if got:
                            act.wait_ge(ip_step, 4 * n + 4)
                            nc.scalar.activation(logs[:, r, :, :], sums[:, r, :, :], ACT.Ln).then_inc(logs_done, 1)
                        for item in items[AHEAD_OF_LOGS[s]:]:
                            if s == 0 and item == items[-1] and prev:
                                probabilities(chunk_at(b, turn, 1, 7, prev, cur), 0)
                            split_hi(b, turn, item)
                        if s == 0 and not cur:
                            probabilities(chunk_at(b, turn, 1, 7, prev, cur), 0)
                        for n in range(ROWS_K, len(W_ROWS)) if first(b) and s == 0 else ():
                            row_hi(n)
                        if not cur and s < DB:
                            if s == 0:
                                act.wait_ge(wo_in, 16 * DB)
                                act.wait_ge(acc_full, item_number(B - 1, ("q", 4)) + 1)
                            nc.scalar.activation(wo_hi[:, s, :], wo_stage[s], ACT.Copy).then_inc(wo_hi_done, 1)
                        if not cur and s == 5:
                            attn_leading(0, 0)

                def attention(chunk):
                    if not chunk:
                        return
                    cb, _, c = chunk
                    act.wait_ge(pv_done, chunk_number(cb, c) + 1)
                    if started(saved_count(cb, c) - 16):
                        act.wait_ge(attn_saved[c % 2], saved_count(cb, c) - 16)
                    nc.scalar.activation(attnT[:, c % 2, :], pv[:, 0:S], ACT.Copy).then_inc(pv_out, 1)

                def probabilities(chunk, t):
                    cb, _, c = chunk
                    g = chunk_number(cb, c)
                    act.wait_ge(scoresT_done, QB * g + t + 1)
                    if t == 0 and first(cb) and c == 0:
                        act.wait_ge(key_rows_in, STACKS)
                    if t == 0 and started(g):
                        act.wait_ge(pv_done, g)
                    nc.scalar.activation(probsT[:, t, :, :], scoresT[:, :, :], ACT.Exp).then_inc(probsT_done, 1)

                def attn_leading(b, odd):
                    act.wait_ge(attn_loaded[odd], 8 * (b - odd) + 16)
                    if started(b - 1):
                        act.wait_ge(out_full, 4 * (b - 1))
                    nc.scalar.activation(attn_hi[odd], attn_in[odd], ACT.Copy).then_inc(attn_hi_done, 1)

                sweep(act, period, apart=1, turns=STACKS)

                def out_period(b, odd, prev, cur):
                    if cur and not first(b):
                        attn_leading(b, odd)
                    if prev:
                        act.wait_ge(out_ready, 4 * b)
                        act.dma_start(in_blocks(out[b - 1]), out_sb[1 - odd]).then_inc(out_saved[1 - odd], 16)

                sweep(act, out_period, apart=3, turns=2)
                for slot in range(2):
                    act.wait_ge(out_saved[slot], 16 * (B // 2))

            @block.vector
            def _(dve):
                def masks(qb):
                    dve.wait_ge(const_in, 32)
                    dve.wait_ge(box_in, 16)
                    step = 7 * qb
                    inside = mask[:, :, qb, BOXES:IP]
                    for k, op in ((0, ALU.is_le), (1, ALU.is_le), (2, ALU.is_ge), (3, ALU.is_ge)):
                        at = grid_sb[:, qb, k % 2:k % 2 + 1]
                        if k == 0:
                            nc.vector.tensor_scalar(inside, box[:, :, :, k], at, None, op).then_inc(mask_step, 1)
                        else:
                            dve.wait_ge(mask_step, step)
                            nc.vector.scalar_tensor_tensor(inside, box[:, :, :, k], at, inside, op, ALU.mult) \
                                .then_inc(mask_step, 1)
                        step += 1
                    dve.wait_ge(mask_step, step)
                    nc.vector.tensor_reduce(any_box[:, qb, :], inside, AX.X, ALU.max).then_inc(mask_step, 1)
                    dve.wait_ge(mask_step, step + 1)
                    nc.vector.tensor_scalar(mask[:, :, qb, 0:BOXES], any_box[:, qb, :].unsqueeze(2).to_broadcast(
                        [P, B, BOXES]), NEG, None, ALU.mult).then_inc(mask_step, 1)
                    nc.vector.tensor_scalar(inside, inside, -NEG, NEG, ALU.mult, ALU.add).then_inc(mask_step, 1)

                def row_lo(n):
                    dve.wait_ge(w_hi, n + 1)
                    nc.vector.tensor_tensor(split_row(n, 1), stage(n), split_row(n, 0).bitcast(F32), ALU.subtract) \
                        .then_inc(w_split, 1)

                for kind, n in SETUP_WORK:
                    if kind == "r":
                        row_lo(n)
                        continue
                    if n >= len(SETUP) - QB:
                        masks(n - len(SETUP) + QB)
                    dve.wait_ge(acc_full, n + 1)
                    if SETUP[n][0] == "v":
                        _, tb, half = SETUP[n]
                        nc.vector.tensor_copy(v[:, tb, half * HALF:(half + 1) * HALF], acc[:, n % RING, 0:HALF]) \
                            .then_inc(acc_free, 1)
                    else:
                        (hi, lo), width = hi_of(SETUP[n])
                        dve.wait_ge(hi_done, min(n, KEYS_IP) + 1)
                        nc.vector.tensor_tensor(lo, acc[:, n % RING, 0:width], hi.bitcast(F32), ALU.subtract) \
                            .then_inc(acc_free, 1)

                def split_lo(b, item):
                    source = acc[:, bank(item), :]
                    if item[0] == "xT" and last(b):
                        return
                    if item[0] == "v":
                        _, tb, half = item
                        rows = P if tb == 0 else TAIL
                        dve.wait_ge(acc_full, item_number(b, item) + 1)
                        if first(b):
                            dve.wait_ge(v_ip_saved, 16)
                        else:
                            dve.wait_ge(pv_done, CHUNKS * b - (CHUNKS // 2 if half == 0 else 0))
                        nc.vector.tensor_copy(v[0:rows, tb, half * HALF:(half + 1) * HALF], source[0:rows, 0:HALF]) \
                            .then_inc(acc_free, 1)
                        return
                    (hi, lo), width = hi_of(item)
                    dve.wait_ge(hi_done, hi_count(b, item))
                    if item[0] == "q":
                        nc.vector.scalar_tensor_tensor(lo, source[:, 0:width], SCALE, hi.bitcast(F32), ALU.mult,
                                                       ALU.subtract).then_inc(acc_free, 1)
                    else:
                        nc.vector.tensor_tensor(lo, source[:, 0:width], hi.bitcast(F32), ALU.subtract) \
                            .then_inc(acc_free, 1)
                    if item[0] == "k":
                        c = item[1]
                        if started(QB * (chunk_number(b, c) - STACKS + 1)):
                            dve.wait_ge(scoresT_done, QB * (chunk_number(b, c) - STACKS + 1))
                        nc.vector.tensor_copy(qk[:, c % 2, 2:4, TEXT:S],
                                              kip[:, c, :, bass.ds(b * IP, IP)].bitcast(F32)).then_inc(kip_copied, 1)

                def period(b, turn, prev, cur):
                    for s in range(STEPS):
                        unit = unit_at(b, turn, s, 4, prev, cur)
                        if unit:
                            ub, _, u = unit
                            n, r = UNITS * ub + u, u % 2
                            dve.wait_ge(scores_done, n + 1)
                            if started(n - 1):
                                dve.wait_ge(shift_step, 3 * (n - 1))
                            nc.vector.tensor_tensor(
                                ip_scores[:, r, :, :], scores[:, :, TEXT:S],
                                mask[:, ub, r, :].unsqueeze(1).to_broadcast([P, HC, IP]), ALU.add).then_inc(ip_step, 1)
                            nc.vector.tensor_reduce(neg_max[:, r, 0, :], scores[:, :, 0:TEXT], AX.X, ALU.max,
                                                    negate=True).then_inc(max_done, 1)
                        if s == 0 and prev:
                            split_lo(b - 1, WORK[-1][-1])
                        items = DVE_WORK[s] if cur else []
                        if s < 2:
                            for item in items[:AHEAD_OF_SUMS[s]]:
                                split_lo(b, item)
                        if unit:
                            dve.wait_ge(ip_step, 4 * n + 1)
                            nc.vector.tensor_reduce(neg_max[:, r, 1, :], ip_scores[:, r, :, :], AX.X, ALU.max,
                                                    negate=True).then_inc(ip_step, 1)
                            dve.wait_ge(ip_step, 4 * n + 2)
                            nc.vector.tensor_tensor(
                                ip_shifted[:, r, :, :], ip_scores[:, r, :, :],
                                neg_max[:, r, 1, :].unsqueeze(2).to_broadcast([P, HC, IP]), ALU.add).then_inc(ip_step, 1)
                        if s >= 2:
                            for item in items[:AHEAD_OF_SUMS[s]]:
                                split_lo(b, item)
                        for n in range(ROWS_K, len(W_ROWS)) if first(b) and s == 1 else ():
                            row_lo(n)
                        got = chunk_at(b, turn, s, 6, prev, cur)
                        if got:
                            cb, ct, c = got
                            dve.wait_ge(shiftsT_done, chunk_number(cb, c) + 1)
                            if started(QB * (chunk_number(cb, c) - STACKS + 1)):
                                dve.wait_ge(scoresT_done, QB * (chunk_number(cb, c) - STACKS + 1))
                            nc.vector.tensor_copy(stacked[ROWS:P, stack_slot(ct, c), :, 0, :],
                                                  shiftsT.unsqueeze(1).to_broadcast([DH, HC, S])).then_inc(shifts_in, 1)
                        if unit:
                            dve.wait_ge(exp_ip_done, n + 1)
                            nc.vector.tensor_reduce(sums[:, r, 1, :], ip_shifted[:, r, :, :], AX.X, ALU.add) \
                                .then_inc(ip_step, 1)
                        for item in items[AHEAD_OF_SUMS[s]:]:
                            split_lo(b, item)
                        if s == 4 and cur:
                            if first(b):
                                dve.wait_ge(shifts_cleared, 1)
                            else:
                                dve.wait_ge(shiftsT_done, CHUNKS * b)
                            nc.vector.tensor_tensor(shifts[:, :, SHIFTS:SHIFTS + IP], mask[:, b, :, :],
                                                    shifts[:, :, SHIFTS + IP:DH].bitcast(F32), ALU.add) \
                                .then_inc(mask_copied, 1)
                        if not cur and s < DB:
                            dve.wait_ge(wo_hi_done, s + 1)
                            nc.vector.tensor_tensor(wo_lo[:, s, :], wo_stage[s], wo_hi[:, s, :].bitcast(F32),
                                                    ALU.subtract).then_inc(wo_split, 1)
                        if not cur and s == 5:
                            attn_rest(0, 0)

                def attn_rest(b, odd):
                    dve.wait_ge(attn_hi_done, b + 1)
                    nc.vector.tensor_tensor(attn_lo[odd], attn_in[odd], attn_hi[odd].bitcast(F32), ALU.subtract) \
                        .then_inc(attn_split, 1)

                sweep(dve, period, apart=1, turns=STACKS)

                def out_period(b, odd, prev, cur):
                    if cur and not first(b):
                        attn_rest(b, odd)
                    if prev:
                        slot, o = 1 - odd, b - 1
                        dve.wait_ge(res_ready, o + 1)
                        if started(8 * (o - slot)):
                            dve.wait_ge(out_saved[slot], 8 * (o - slot))
                        for n in range(4):
                            at = (slice(None), n // 2, slice(n % 2 * HALF, (n % 2 + 1) * HALF))
                            dve.wait_ge(out_full, 4 * o + n + 1)
                            nc.vector.tensor_tensor(out_sb[slot][at], out_acc[n], residual[slot][at], ALU.add) \
                                .then_inc(out_ready, 1)

                sweep(dve, out_period, apart=3, turns=2)

            @block.tensor
            def _(pe):
                def three_passes(to, stationary, moving, blocks, done, late=None, meanwhile=None):
                    for n in range(blocks):
                        if meanwhile and n == meanwhile[0]:
                            meanwhile[1]()
                        if late and n in late[1]:
                            pe.wait_ge(late[0], late[1][n])
                        for s_part, m_part in ((0, 0), (0, 1), (1, 0)):
                            mm = nc.tensor.matmul(to, stationary(s_part, n), moving(m_part, n),
                                                  start=(n == 0 and s_part == 0 and m_part == 0),
                                                  stop=(n == blocks - 1 and s_part == 1))
                    mm.then_inc(done, 1)

                def run_item(item, to, late=None, meanwhile=None):
                    kind = item[0]
                    if kind in ("xT", "ctxT"):
                        source, blocks = (x_in, DB) if kind == "xT" else (ctx_in, CB)
                        g = item[1]
                        for blk in range(2 * g, min(2 * g + 2, blocks)):
                            for t in range(QB):
                                at = ((blk - 2 * g) * QB + t) * P
                                mm = nc.tensor.transpose(to[:, at:at + P], source[:, t, blk * P:(blk + 1) * P],
                                                         ident_sb[:, :])
                        mm.then_inc(acc_full, 1)
                    elif kind == "q":
                        cols = slice(item[1] * P, (item[1] + 1) * P)
                        three_passes(to[:, 0:S], lambda part, n: (wq_hi, wq_lo)[part][:, n, cols],
                                     lambda part, n: (xT_hi, xT_lo)[part][:, n, :], DB, acc_full, late)
                    elif kind in ("k", "k_ip"):
                        cols = slice(item[1] * P, (item[1] + 1) * P)
                        width = TEXT if kind == "k" else B * IP
                        three_passes(to[:, 0:width], lambda part, n: (wk_hi, wk_lo)[part][:, n, cols],
                                     lambda part, n: (cT_hi, cT_lo)[part][:, n, 0:width], CB, acc_full, late, meanwhile)
                    else:
                        _, tb, half = item
                        three_passes(to[:, 0:HALF], lambda part, n: (cT_hi, cT_lo)[part][:, n, tb * P:(tb + 1) * P],
                                     lambda part, n: (wv_hi, wv_lo)[part][:, n, half * HALF:(half + 1) * HALF],
                                     CB, acc_full, late, meanwhile)

                pe.wait_ge(const_in, 32)
                for n, item in enumerate(SETUP):
                    if item == ("ctxT", 0):
                        pe.wait_ge(ctx_ip_loaded, 16 * QB)
                    if item == ("xT", 0):
                        pe.wait_ge(x_loaded, 16)
                    late = (w_split, {r: r + 1 for r in range(CB)}) if item == ("k_ip", 0) else None
                    if item == ("v", 0, 0):
                        pe.wait_ge(w_split, ROWS_V_IP)
                    if n >= RING:
                        pe.wait_ge(acc_free, n - RING + 1)
                    run_item(item, acc[:, n % RING, :], late)

                def project(b, item, meanwhile=None):
                    n = item_number(b, item)
                    if item[0] == "xT" and last(b):
                        return
                    pe.wait_ge(acc_free, n - RING + 1)
                    if item == ("ctxT", 0):
                        pe.wait_ge(ctx_loaded, 16 * (b + 1))
                    if item == ("xT", 0):
                        pe.wait_ge(x_loaded, 16 * (b + 2))
                    late = None
                    if item == ("q", 0) and not first(b):
                        late = (acc_free, {DB - 1: item_number(b - 1, ("xT", 2)) + 1})
                    if item == ("k", 0):
                        late = (acc_free, {2 * g: item_number(b, ("ctxT", g)) + 1 for g in range(4)})
                    if first(b) and item in (("q", 0), ("k", 0)):
                        pe.wait_ge(w_split, {"q": ROWS_Q, "k": ROWS_K}[item[0]])
                    if first(b) and item == ("v", 0, 0):
                        late = (w_split, {r: ROWS_K + r + 1 for r in range(CB)})
                    run_item(item, acc[:, bank(item), :], late, meanwhile)

                def values(chunk):
                    if not chunk:
                        return
                    cb, _, c = chunk
                    g = chunk_number(cb, c)
                    pe.wait_ge(probsT_done, QB * (g + 1))
                    if c in (0, CHUNKS // 2):
                        pe.wait_ge(acc_free, item_number(cb, ("v", 1, 0 if c == 0 else 1)) + 1)
                    if c == 0:
                        pe.wait_ge(v_ip_loaded, 16 * (cb + 1))
                    if started(g):
                        pe.wait_ge(pv_out, g)
                    for t in range(QB):
                        for h in range(HC):
                            col = (HC * c + h) * DH
                            mm = nc.tensor.matmul(pv[DH * h:DH * (h + 1), 0:S], v[:, t, col:col + DH],
                                                  probsT[:, t, h, :], start=(t == 0), stop=(t == QB - 1))
                    mm.then_inc(pv_done, 1)

                def transposed_shifts(chunk):
                    if not chunk:
                        return
                    cb, _, c = chunk
                    g = chunk_number(cb, c)
                    pe.wait_ge(shift_step, 3 * UNITS // CHUNKS * (g + 1))
                    if c == 0:
                        pe.wait_ge(mask_copied, cb + 1)
                    if started(g):
                        pe.wait_ge(probsT_done, QB * g)
                    for t in range(QB):
                        mm = nc.tensor.matmul(shiftsT[:, t * P:(t + 1) * P], shifts[:, t, :].bitcast(F32),
                                              ident_sb[:, :], start=True, stop=True)
                    mm.then_inc(shiftsT_done, 1)

                def unit_scores(unit):
                    if not unit:
                        return
                    ub, ut, u = unit
                    n, slot = UNITS * ub + u, stack_slot(ut, u // 2)
                    if u % 2 == 0:
                        pe.wait_ge(stack_in[slot], stack_count(ub, ut, u // 2))
                    if started(n):
                        pe.wait_ge(exp_done, n)
                    for h in range(HC):
                        mm = nc.tensor.matmul(scores[:, h, :],
                                              stacked[0:ROWS, slot, h, 0, (u % 2) * P:(u % 2 + 1) * P],
                                              stacked[0:ROWS, slot, h, 1, :], start=True, stop=True)
                    mm.then_inc(scores_done, 1)

                def transposed_scores(chunk, t):
                    if not chunk:
                        return
                    cb, ct, c = chunk
                    g, slot = chunk_number(cb, c), stack_slot(ct, c)
                    if t == 0:
                        pe.wait_ge(shifts_in, g + 1)
                        if first(cb) and c < STACKS:
                            pe.wait_ge(key_rows_in, STACKS)
                    if started(QB * g + t):
                        pe.wait_ge(probsT_done, QB * g + t)
                    for h in range(HC):
                        mm = nc.tensor.matmul(scoresT[:, h, :], stacked[:, slot, h, 1, t * P:(t + 1) * P],
                                              stacked[:, slot, h, 0, :], start=True, stop=True)
                    mm.then_inc(scoresT_done, 1)

                def period(b, turn, prev, cur):
                    for s in range(STEPS):
                        transposed = chunk_at(b, turn, s, 7, prev, cur)
                        if s != 1:
                            transposed_scores(transposed, 0)
                        items = WORK[s] if cur else []
                        done, shifted = chunk_at(b, turn, s, 8, prev, cur), chunk_at(b, turn, s, 6, prev, cur)
                        if items == [("v", 0, 0)]:
                            project(b, items[0], (3, lambda: (values(done), transposed_shifts(shifted))))
                        else:
                            values(done)
                            transposed_shifts(shifted)
                        if items == [("k", 0)]:
                            project(b, items[0], (CB // 2, lambda: transposed_scores(transposed, 1)))
                        elif items != [("v", 0, 0)]:
                            for item in items[:1]:
                                project(b, item)
                            transposed_scores(transposed, 1)
                            for item in items[1:-1]:
                                project(b, item)
                        if s == 0:
                            unit_scores(unit_at(b, turn, s, 3, prev, cur))
                            transposed_scores(chunk_at(b, turn, 1, 7, prev, cur), 0)
                        for item in items[1:][-1:]:
                            project(b, item)
                        if s > 0:
                            unit_scores(unit_at(b, turn, s, 3, prev, cur))

                sweep(pe, period, apart=1, turns=STACKS)
                pe.wait_ge(wo_split, DB)
                pe.wait_ge(exp_done, UNITS * B)

                def out_period(b, odd, prev, cur):
                    if not cur:
                        return
                    pe.wait_ge(attn_split, b + 1)
                    for n in range(4):
                        t, half = n // 2, n % 2
                        if started(b):
                            pe.wait_ge(out_ready, 4 * (b - 1) + n + 1)
                        three_passes(
                            out_acc[n],
                            lambda part, c: (attn_hi, attn_lo)[part][odd][:, c * S + t * P:c * S + (t + 1) * P],
                            lambda part, c: (wo_hi, wo_lo)[part][:, c, half * HALF:(half + 1) * HALF], DB, out_full)

                sweep(pe, out_period, apart=3, turns=2)


def _grid(side, blocks):
    import numpy as np
    step = np.arange(side - 1, dtype=np.float32) * np.float32(1 / (side - 1))
    line = np.concatenate([step, np.ones(1, np.float32)])
    n = np.arange(side * side)
    both = np.stack([line[n % side], line[n // side]], axis=-1)
    return np.ascontiguousarray(both.reshape(blocks, -1, 2).transpose(1, 0, 2))


def _key_rows(heads, rows, keys, ip):
    import numpy as np
    shifts = np.zeros((2, 2, heads, heads, keys), np.float32)
    for h in range(heads):
        shifts[0, :, h, h, :keys - ip] = 1
        shifts[1, :, h, h, keys - ip:] = 1
    out = np.zeros((rows, heads, keys), np.float32)
    out[:4 * heads] = shifts.reshape(4 * heads, heads, keys)
    for m in range(ip):
        out[4 * heads + m, :, keys - ip + m] = 1
    return out


_INS = ['x', 'ctx_2048', 'fside_Bx4x4_0', 'L0_xattn_w_q', 'L0_xattn_w_k', 'L0_xattn_w_v', 'L0_xattn_w_k_ip',
        'L0_xattn_w_v_ip', 'L0_xattn_w_out', 'L0_xattn_b_out']


def kernel(**inputs):
    import numpy as _np
    import concourse.bacc as _bacc
    from concourse import mybir as _mybir
    from concourse.bass_utils import run_bass_kernel_spmd as _run

    nc = _bacc.Bacc("TRN2", target_bir_lowering=False, num_devices=1)
    arrays, args = {}, []
    given = {name: _np.ascontiguousarray(inputs[name]) for name in _INS}
    given["grid"] = _grid(16, 2)
    given["ident"] = _np.eye(128, dtype=_np.float32)
    given["key_rows"] = _key_rows(4, 32, 256, 8)
    for name, a in given.items():
        arrays[f"in_{name}_dram"] = a
        args.append(nc.dram_tensor(f"in_{name}_dram", a.shape, _mybir.dt.from_np(a.dtype), kind="ExternalInput").ap())
    shape = given["x"].shape
    args.append(nc.dram_tensor("out_0_dram", shape, _mybir.dt.float32, kind="ExternalOutput").ap())
    decoupled_cross_attention(nc, *args)
    r = _run(nc, [arrays], core_ids=[0])
    return r.results[0]["out_0_dram"]
```
